# Optimizing a Trainium2 kernel written in Bass

```python
import numpy as np
import jax
import jax.numpy as jnp

def _softmax(x, axis=-1):
    return jax.nn.softmax(x, axis=axis)

def _gelu(x):
    return jax.nn.gelu(x, approximate=True)

def _silu(x):
    return jax.nn.silu(x)

def _sigmoid(x):
    return jax.nn.sigmoid(x)

def _layernorm(x, axis=-1, eps=1e-05):
    m = jnp.mean(x, axis=axis, keepdims=True)
    v = jnp.var(x, axis=axis, keepdims=True)
    return (x - m) / jnp.sqrt(v + eps)

def _scatter_add(tgt, idx, src, axis=0):
    return tgt.at[idx].add(src)

def _segment_sum(src, seg, n):
    return jax.ops.segment_sum(src, seg, n)
kernel_name = 'mk_cond_resid_d2_seqx_r4_f39e4c'

def setup_inputs(seed: int=0):
    np.random.seed(seed)
    _w = jnp.asarray

    def _rec_inputs():
        import jax
        import jax.numpy as jnp
        _rk = jax.random.key(seed)
        x = 7.22e-05 + 1 * jax.random.normal(jax.random.fold_in(_rk, 1), (2, 1024, 256), jnp.float32)
        _lenS = 1024 - jax.random.randint(jax.random.fold_in(_rk, 7), (2,), 0, max(1, 1024 // 4) + 1, jnp.int32)
        _lenS2 = 1024 - jax.random.randint(jax.random.fold_in(_rk, 8), (2,), 0, max(1, 1024 // 4) + 1, jnp.int32)
        cond_8 = -0.104238 + 1.01173 * jax.random.normal(jax.random.fold_in(_rk, 11), (2, 8), jnp.float32)
        return (x, cond_8)
    x, cond_8 = _rec_inputs()

    def _L0_cond_setup():
        import jax, jax.numpy as jnp
        import numpy as np
        TOP_K = 2
        NUM_MOE_LAYERS = 12

        def _gemma_mlp(x, gate_w, up_w, down_w):
            g = jnp.einsum('bsh,hi->bsi', x, gate_w)
            u = jnp.einsum('bsh,hi->bsi', x, up_w)
            return jnp.einsum('bsi,ih->bsh', jax.nn.gelu(g, approximate=True) * u, down_w)
        key = jax.random.key(seed)
        ks = jax.random.split(key, 8)
        B, S, H, I, E = (32, 64, 256, 1024, 8)
        std = 0.02
        return {'x': jax.random.normal(ks[0], (B, S, H), jnp.float32), 'router_logits': jax.random.normal(ks[1], (B, E), jnp.float32), 'skill_gate': jax.random.normal(ks[2], (E, H, I), jnp.float32) * std, 'skill_up': jax.random.normal(ks[3], (E, H, I), jnp.float32) * std, 'skill_down': jax.random.normal(ks[4], (E, I, H), jnp.float32) * std, 'shared_gate': jax.random.normal(ks[5], (H, I), jnp.float32) * std, 'shared_up': jax.random.normal(ks[6], (H, I), jnp.float32) * std, 'shared_down': jax.random.normal(ks[7], (I, H), jnp.float32) * std}
    _L0_cond_all = _L0_cond_setup()
    _L0_cond_in = {k: v for k, v in _L0_cond_all.items() if k in ('skill_gate', 'skill_up', 'skill_down', 'shared_gate', 'shared_up', 'shared_down')}
    del _L0_cond_all

    def _L1_cond_setup():
        import jax, jax.numpy as jnp
        import numpy as np
        R = 16
        ALPHA = 32.0
        SCALING = ALPHA / R
        key = jax.random.key(seed)
        ks = jax.random.split(key, 6)
        B, T, C, O, E = (16, 375, 256, 256, 8)
        x = jax.random.normal(ks[0], (B, T, C), dtype=jnp.float32)
        w = jax.random.uniform(ks[1], (B, E), dtype=jnp.float32)
        W_base = jax.random.normal(ks[2], (O, C), dtype=jnp.float32) * 0.02
        b_base = jax.random.normal(ks[3], (O,), dtype=jnp.float32) * 0.02
        As = jax.random.normal(ks[4], (E, R, C), dtype=jnp.float32) * 0.02
        Bs = jax.random.normal(ks[5], (E, O, R), dtype=jnp.float32) * 0.02
        return {'x': x, 'w': w, 'W_base': W_base, 'b_base': b_base, 'As': As, 'Bs': Bs}
    _L1_cond_all = _L1_cond_setup()
    _L1_cond_in = {k: v for k, v in _L1_cond_all.items() if k in ('W_base', 'b_base', 'As', 'Bs')}
    del _L1_cond_all
    return {'x': x, 'cond_8': cond_8, 'L0_cond_skill_gate': _L0_cond_in['skill_gate'], 'L0_cond_skill_up': _L0_cond_in['skill_up'], 'L0_cond_skill_down': _L0_cond_in['skill_down'], 'L0_cond_shared_gate': _L0_cond_in['shared_gate'], 'L0_cond_shared_up': _L0_cond_in['shared_up'], 'L0_cond_shared_down': _L0_cond_in['shared_down'], 'L1_cond_W_base': _L1_cond_in['W_base'], 'L1_cond_b_base': _L1_cond_in['b_base'], 'L1_cond_As': _L1_cond_in['As'], 'L1_cond_Bs': _L1_cond_in['Bs']}

def reference(x, cond_8, L0_cond_skill_gate, L0_cond_skill_up, L0_cond_skill_down, L0_cond_shared_gate, L0_cond_shared_up, L0_cond_shared_down, L1_cond_W_base, L1_cond_b_base, L1_cond_As, L1_cond_Bs):
    import jax
    import jax.numpy as jnp

    def _L0_cond_ref(x, router_logits, skill_gate, skill_up, skill_down, shared_gate, shared_up, shared_down):
        import jax, jax.numpy as jnp
        import numpy as np
        TOP_K = 2
        NUM_MOE_LAYERS = 12

        def _gemma_mlp(x, gate_w, up_w, down_w):
            g = jnp.einsum('bsh,hi->bsi', x, gate_w)
            u = jnp.einsum('bsh,hi->bsi', x, up_w)
            return jnp.einsum('bsi,ih->bsh', jax.nn.gelu(g, approximate=True) * u, down_w)
        B = x.shape[0]
        E = skill_gate.shape[0]
        rw = jax.nn.softmax(router_logits.astype(jnp.float32), axis=-1)
        w, sel = jax.lax.top_k(rw, TOP_K)
        w = w / w.sum(axis=-1, keepdims=True)
        w = w.astype(x.dtype)
        scale = 1.0 / NUM_MOE_LAYERS
        w = scale * w + (1.0 - scale) * jax.lax.stop_gradient(w)
        dense_w = jnp.zeros((B, E), x.dtype).at[jnp.arange(B)[:, None], sel].add(w)

        def step(acc, params):
            g, u, d, we = params
            return (acc + we[:, None, None] * _gemma_mlp(x, g, u, d), None)
        out, _ = jax.lax.scan(step, jnp.zeros_like(x), (skill_gate, skill_up, skill_down, dense_w.T))
        out = out + _gemma_mlp(x, shared_gate, shared_up, shared_down)
        return out

    def _L1_cond_ref(x, w, W_base, b_base, As, Bs):
        import jax, jax.numpy as jnp
        import numpy as np
        R = 16
        ALPHA = 32.0
        SCALING = ALPHA / R
        out = jnp.einsum('btc,oc->bto', x, W_base) + b_base
        h = jnp.einsum('btc,erc->bter', x, As)
        lora = jnp.einsum('bter,eor,be->bto', h, Bs, w)
        return out + lora * SCALING
    x = x + _L0_cond_ref(x, cond_8, L0_cond_skill_gate, L0_cond_skill_up, L0_cond_skill_down, L0_cond_shared_gate, L0_cond_shared_up, L0_cond_shared_down)
    x = x + _L1_cond_ref(x, cond_8, L1_cond_W_base, L1_cond_b_base, L1_cond_As, L1_cond_Bs)
    return x

_drawn_inputs = setup_inputs


def setup_inputs(seed=0):
    import zlib

    import numpy as np

    out = dict(_drawn_inputs(seed))
    spreads = {}
    factors = {'L1_cond_b_base': 3.283}
    for name, (base, spread) in spreads.items():
        noise = np.random.default_rng([zlib.crc32(name.encode()), seed]).standard_normal(out[name].shape)
        drawn = base * np.exp(spread * noise) if base else spread * noise
        out[name] = jnp.asarray(drawn.astype(out[name].dtype))
    for name, factor in factors.items():
        out[name] = (out[name] * factor).astype(out[name].dtype)
    return out
```

```python
import concourse.bass as bass
from concourse import mybir
from contextlib import ExitStack


def moe_lora_program(nc, x, cond, skill_gate, skill_up, skill_down, shared_gate, shared_up,
                     shared_down, w_base, b_base, lora_a, lora_b, out):
    F32 = mybir.dt.float32
    F32R = mybir.dt.float32r
    U32 = mybir.dt.uint32
    ALU = mybir.AluOpType
    ACT = mybir.ActivationFunctionType
    AX_X = mybir.AxisListType.X

    P = 128
    B, S, H = x.shape
    E, _, I = skill_gate.shape
    R = lora_a.shape[1]
    KC = H // P
    HALF = 512
    HALVES = S // HALF
    TILES = HALF // P
    QUARTERS = 4
    IQ = I // QUARTERS
    CQ = IQ // P
    TOP_K = 2
    NUM_MOE_LAYERS = 12
    GRAD_SCALE = 1.0 / NUM_MOE_LAYERS
    LORA_SCALING = 32.0 / R
    SEGMENTS = B * (TOP_K + 1)
    SEG_PER_BATCH = TOP_K + 1
    UNITS_Q = CQ * HALVES
    UNITS = QUARTERS * UNITS_Q
    GU = 2 * KC * IQ
    DN = CQ * H
    BSTEP = KC * S
    JOBS_BEFORE_LOOP = B * HALVES + UNITS_Q
    LIN_TURN_AT = 2 * UNITS_Q
    LIN_MIX_AT = LIN_TURN_AT + 1
    SMALL_LOADS = 1 + KC + 2 + B * E

    ctx = ExitStack()
    with ctx:
        def sb(name, shape, dt=F32):
            return ctx.enter_context(nc.sbuf_tensor(name, shape, dt))

        def sem(name):
            return ctx.enter_context(nc.semaphore(name))

        x_rows = sb("x_rows", [P, B, HALVES, TILES, H])
        x_t = sb("x_t", [P, B * KC * S])
        x_hi = sb("x_hi", [P, B * KC * S], F32R)
        x_lo = sb("x_lo", [P, B * KC * S], F32R)
        gu_stage = sb("gu_stage", [P, QUARTERS, 2, KC, IQ])
        dn_stage = sb("dn_stage", [P, QUARTERS, CQ, H])
        gu_hi = sb("gu_hi", [P, QUARTERS, 2, KC, IQ], F32R)
        gu_lo = sb("gu_lo", [P, QUARTERS, 2, KC, IQ], F32R)
        dn_hi = sb("dn_hi", [P, QUARTERS, CQ, H], F32R)
        dn_lo = sb("dn_lo", [P, QUARTERS, CQ, H], F32R)
        gelu = sb("gelu", [P, 2, HALF])
        prod = sb("prod", [P, 2, HALF])
        h_hi = sb("h_hi", [P, 2, HALF], F32R)
        h_lo = sb("h_lo", [P, 2, HALF], F32R)
        ident = sb("ident", [P, P])
        wb_rows = sb("wb_rows", [P, KC, H])
        lb_rows = sb("lb_rows", [P, KC, E, R])
        la_sb = sb("la_sb", [P, H])
        bias = sb("bias", [P, H])
        lora_w = sb("lora_w", [P, B])
        wb_t = sb("wb_t", [P, KC, H])
        lb_t = sb("lb_t", [P, B, H])
        lin = sb("lin", [P, B, KC, H])
        lin_hi = sb("lin_hi", [P, B, KC, H], F32R)
        lin_lo = sb("lin_lo", [P, B, KC, H], F32R)
        logits = sb("logits", [P, B, E])
        top = sb("top", [P, B])
        shifted = sb("shifted", [P, B, E])
        expo = sb("expo", [P, B, E])
        total = sb("total", [P, B])
        inv_total = sb("inv_total", [P, B])
        probs = sb("probs", [P, B, E])
        best = sb("best", [P, B, 8])
        best_at = sb("best_at", [P, B, 8], U32)
        pair_sum = sb("pair_sum", [P, B])
        inv_pair = sb("inv_pair", [P, B])
        norm_w = sb("norm_w", [P, B, TOP_K])
        scaled_w = sb("scaled_w", [P, B, TOP_K])
        seg_w = sb("seg_w", [P, SEGMENTS])
        chosen = sb("chosen", [1, B * TOP_K], U32)

        gate_ps = [ctx.enter_context(nc.psum_tensor(f"gate_ps{i}", [P, HALF], F32)) for i in range(2)]
        up_ps = [ctx.enter_context(nc.psum_tensor(f"up_ps{i}", [P, HALF], F32)) for i in range(2)]
        sum_ps = [[ctx.enter_context(nc.psum_tensor(f"sum_ps{h}{m}", [P, HALF], F32))
                   for m in range(KC)] for h in range(HALVES)]

        x_in = [[sem(f"x_in{b}{h}") for h in range(HALVES)] for b in range(B)]
        gu_in = [sem(f"gu_in{q}") for q in range(QUARTERS)]
        dn_in = [sem(f"dn_in{q}") for q in range(QUARTERS)]
        logits_in = sem("logits_in")
        small_in = sem("small_in")
        seg_one = sem("seg_one")
        ident_zero = sem("ident_zero")
        ident_ready = sem("ident_ready")
        route_step = sem("route_step")
        shift_ready = sem("shift_ready")
        exp_ready = sem("exp_ready")
        routed = sem("routed")
        x_turned = sem("x_turned")
        x_hi_ready = sem("x_hi_ready")
        x_t_ready = sem("x_t_ready")
        x_split = sem("x_split")
        gu_hi_ready = sem("gu_hi_ready")
        gu_split = sem("gu_split")
        dn_hi_ready = sem("dn_hi_ready")
        dn_split = sem("dn_split")
        gate_ready = sem("gate_ready")
        up_ready = sem("up_ready")
        gelu_ready = sem("gelu_ready")
        prod_ready = sem("prod_ready")
        h_hi_ready = sem("h_hi_ready")
        h_split = sem("h_split")
        down_done = sem("down_done")
        sum_taken = sem("sum_taken")
        lin_turned = sem("lin_turned")
        lin_t_ready = sem("lin_t_ready")
        wb_copied = sem("wb_copied")
        lin_mixed = sem("lin_mixed")
        lin_ready = sem("lin_ready")
        lin_hi_ready = sem("lin_hi_ready")
        lin_split = sem("lin_split")
        y_hi_ready = sem("y_hi_ready")
        y_split = sem("y_split")
        y_split_last = sem("y_split_last")
        out_ps_ready = sem("out_ps_ready")
        out_ready = sem("out_ready")
        out_stored = sem("out_stored")

        def unit_at(k):
            return k // UNITS_Q, k % UNITS_Q // HALVES, k % HALVES

        def x_cols(b, kc, half):
            return b * BSTEP + kc * S + half * HALF

        def halves_view(tile, b, half):
            return tile[:, b * BSTEP:(b + 1) * BSTEP].rearrange("p (k s) -> p k s", k=KC)[
                :, :, half * HALF:(half + 1) * HALF]

        x_dram = x.rearrange("b (h p t) c -> b h p t c", h=HALVES, t=TILES)
        out_dram = out.rearrange("b (h p t) c -> b h p t c", h=HALVES, t=TILES)

        block = ctx.enter_context(nc.Block())

        @block.sync
        def _(sp):
            def load_x(b, half):
                sp.dma_start(x_rows[:, b, half], x_dram[b, half]).then_inc(x_in[b][half], 16)

            def load_quarter(gate, up, down, slot):
                cols = slice(slot * IQ, (slot + 1) * IQ)
                for m, w in enumerate((gate, up)):
                    sp.dma_start(gu_stage[:, slot, m],
                                 w[:, cols].rearrange("(k p) n -> p k n", p=P)).then_inc(gu_in[slot], 16)
                sp.dma_start(dn_stage[:, slot],
                             down[cols, :].rearrange("(c p) n -> p c n", p=P)).then_inc(dn_in[slot], 16)

            load_x(0, 0)
            load_quarter(shared_gate, shared_up, shared_down, 0)
            load_x(0, 1)
            load_quarter(shared_gate, shared_up, shared_down, 1)
            load_x(1, 0)
            load_x(1, 1)
            load_quarter(shared_gate, shared_up, shared_down, 2)
            load_quarter(shared_gate, shared_up, shared_down, 3)
            sp.wait_ge(routed, 1)
            with sp.Fori(1, SEGMENTS - 1) as s:
                e = sp.value_load(chosen[0:1, bass.ds(s - 1, 1)], min_val=0, max_val=E - 1)
                for q in range(QUARTERS):
                    sp.wait_ge(gu_split, QUARTERS * s + q - QUARTERS + 1)
                    sp.wait_ge(dn_split, QUARTERS * s + q - QUARTERS + 1)
                    gate = skill_gate[bass.ds(e, 1)].rearrange("e h i -> (e h) i")
                    up = skill_up[bass.ds(e, 1)].rearrange("e h i -> (e h) i")
                    down = skill_down[bass.ds(e, 1)].rearrange("e i h -> (e i) h")
                    load_quarter(gate, up, down, q)
            for q in range(QUARTERS):
                done = QUARTERS * (SEGMENTS - 2) + q + 1
                sp.wait_ge(gu_split, done)
                sp.wait_ge(dn_split, done)
                load_quarter(shared_gate, shared_up, shared_down, q)
            stored = 0
            for b in range(B):
                for half in range(HALVES):
                    for j in range(TILES // 2):
                        stored += 1
                        sp.wait_ge(out_ready, stored)
                        sp.dma_start(out_dram[b, half, :, 2 * j:2 * j + 2],
                                     x_rows[:, b, half, 2 * j:2 * j + 2]).then_inc(out_stored, 16)
            sp.wait_ge(out_stored, 16 * stored)

        @block.gpsimd
        def _(pool):
            nc.gpsimd.memset(ident[:], 0.0).then_inc(ident_zero, 1)
            nc.gpsimd.memset(seg_w[:], 1.0).then_inc(seg_one, 1)
            pool.wait_ge(ident_zero, 1)
            nc.gpsimd.affine_select(out=ident[:], in_=ident[:], compare_op=ALU.not_equal, fill=1.0,
                                    base=0, pattern=[[-1, P]], channel_multiplier=1
                                    ).then_inc(ident_ready, 1)
            pool.dma_start(wb_rows[:], w_base.rearrange("(k p) c -> p k c", p=P)).then_inc(small_in, 16)
            for k in range(KC):
                pool.dma_start(lb_rows[:, k], lora_b[:, k * P:(k + 1) * P, :].rearrange("e p r -> p e r")
                               ).then_inc(small_in, 16)
            pool.dma_start(la_sb[:], lora_a.rearrange("e r c -> (e r) c")).then_inc(small_in, 16)
            pool.dma_start(bias[:], b_base.partition_broadcast(P)
                           ).then_inc(small_in, 16)
            for b in range(B):
                for e in range(E):
                    pool.dma_start(lora_w[e * R:(e + 1) * R, b:b + 1],
                                   cond[b, e:e + 1].partition_broadcast(R)).then_inc(small_in, 16)

            def lo_part(n, slot):
                pool.wait_ge(gu_hi_ready, n + 1)
                nc.gpsimd.tensor_tensor(gu_lo[:, slot], gu_stage[:, slot], gu_hi[:, slot].bitcast(F32),
                                        ALU.subtract).then_inc(gu_split, 1)
                pool.wait_ge(dn_hi_ready, n + 1)
                nc.gpsimd.tensor_tensor(dn_lo[:, slot], dn_stage[:, slot], dn_hi[:, slot].bitcast(F32),
                                        ALU.subtract).then_inc(dn_split, 1)

            for n in range(QUARTERS):
                lo_part(n, n)
            with pool.Fori(1, SEGMENTS) as s:
                for q in range(QUARTERS):
                    lo_part(QUARTERS * s + q, q)
            for half in range(HALVES):
                pool.wait_ge(y_hi_ready, half + 1)
                nc.gpsimd.tensor_tensor(halves_view(x_lo, 0, half), halves_view(x_t, 0, half),
                                        halves_view(x_hi, 0, half).bitcast(F32), ALU.subtract
                                        ).then_inc(y_split, 1)
            pool.wait_ge(lin_hi_ready, 1)
            nc.gpsimd.tensor_tensor(lin_lo[:], lin[:], lin_hi[:].bitcast(F32), ALU.subtract
                                    ).then_inc(lin_split, 1)

        @block.scalar
        def _(act):
            act.dma_start(logits[:], cond.partition_broadcast(P)).then_inc(logits_in, 16)
            act.wait_ge(shift_ready, 1)
            nc.scalar.activation(expo[:], shifted[:], ACT.Exp).then_inc(exp_ready, 1)

            def x_hi_part(b, half, job):
                for kc in range(KC):
                    act.wait_ge(x_t_ready, KC * job + kc + 1)
                    at = x_cols(b, kc, half)
                    nc.scalar.activation(x_hi[:, at:at + HALF], x_t[:, at:at + HALF], ACT.Copy
                                         ).then_inc(x_hi_ready, 1)

            def gu_hi_part(n, slot, fill):
                act.wait_ge(gu_in[slot], 32 * fill)
                nc.scalar.activation(gu_hi[:, slot], gu_stage[:, slot], ACT.Copy).then_inc(gu_hi_ready, 1)

            def dn_hi_part(n, slot, fill):
                act.wait_ge(dn_in[slot], 16 * fill)
                nc.scalar.activation(dn_hi[:, slot], dn_stage[:, slot], ACT.Copy).then_inc(dn_hi_ready, 1)

            def gelu_part(unit, k):
                act.wait_ge(gate_ready, unit + 1)
                nc.scalar.activation(gelu[:, k % 2], gate_ps[k % 2][:], ACT.Gelu_apprx_tanh
                                     ).then_inc(gelu_ready, 1)

            def h_hi_part(unit, k):
                act.wait_ge(prod_ready, unit + 1)
                nc.scalar.activation(h_hi[:, k % 2], prod[:, k % 2], ACT.Copy).then_inc(h_hi_ready, 1)

            x_hi_part(0, 0, 0)
            gu_hi_part(0, 0, 1)
            x_hi_part(0, 1, 1)
            dn_hi_part(0, 0, 1)
            gu_hi_part(1, 1, 1)
            dn_hi_part(1, 1, 1)
            for k in range(UNITS_Q):
                gelu_part(k, k)
                h_hi_part(k, k)
                if k == 1:
                    gu_hi_part(2, 2, 1)
                    dn_hi_part(2, 2, 1)
            gu_hi_part(3, 3, 1)
            x_hi_part(1, 0, 2)
            x_hi_part(1, 1, 3)
            dn_hi_part(3, 3, 1)
            with act.Fori(0, SEGMENTS - 1) as s:
                for q in range(1, QUARTERS):
                    for j in range(UNITS_Q):
                        k = q * UNITS_Q + j
                        gelu_part(UNITS * s + k, k)
                        h_hi_part(UNITS * s + k, k)
                        if j == 1:
                            act.wait_ge(down_done, UNITS * s + q * UNITS_Q)
                            gu_hi_part(QUARTERS * (s + 1) + q - 1, q - 1, s + 2)
                        if j == 2:
                            dn_hi_part(QUARTERS * (s + 1) + q - 1, q - 1, s + 2)
                for k in range(UNITS_Q):
                    gelu_part(UNITS * (s + 1) + k, k)
                    h_hi_part(UNITS * (s + 1) + k, k)
                    if k == 1:
                        act.wait_ge(down_done, UNITS * (s + 1))
                        gu_hi_part(QUARTERS * (s + 1) + QUARTERS - 1, QUARTERS - 1, s + 2)
                    if k == 2:
                        dn_hi_part(QUARTERS * (s + 1) + QUARTERS - 1, QUARTERS - 1, s + 2)
            s = SEGMENTS - 1
            jobs = JOBS_BEFORE_LOOP + UNITS * (SEGMENTS - 1)
            for k in range(UNITS_Q, UNITS):
                if k == LIN_TURN_AT or k == LIN_MIX_AT:
                    jobs += 1
                act.wait_ge(gate_ready, UNITS * s + k + 1)
                nc.scalar.activation(gelu[:, k % 2], gate_ps[jobs % 2][:], ACT.Gelu_apprx_tanh
                                     ).then_inc(gelu_ready, 1)
                jobs += 1
                h_hi_part(UNITS * s + k, k)
                if k in (UNITS_Q, UNITS_Q + 1):
                    half = k - UNITS_Q
                    act.wait_ge(sum_taken, HALVES * SEG_PER_BATCH)
                    nc.scalar.activation(halves_view(x_hi, 0, half), halves_view(x_t, 0, half), ACT.Copy
                                         ).then_inc(y_hi_ready, 1)
                if k == LIN_MIX_AT + 1:
                    act.wait_ge(lin_ready, 1)
                    nc.scalar.activation(lin_hi[:], lin[:], ACT.Copy).then_inc(lin_hi_ready, 1)
            for half in range(HALVES):
                act.wait_ge(sum_taken, HALVES * (SEGMENTS - 1) + half + 1)
                nc.scalar.activation(halves_view(x_hi, 1, half), halves_view(x_t, 1, half), ACT.Copy
                                     ).then_inc(y_hi_ready, 1)

        @block.vector
        def _(dve):
            steps = [0]

            def after(instruction):
                steps[0] += 1
                instruction.then_inc(route_step, 1)
                dve.wait_ge(route_step, steps[0])

            dve.wait_ge(logits_in, 16)
            after(nc.vector.reduce_max(top[:], logits[:], AX_X))
            nc.vector.tensor_tensor(shifted[:], logits[:], top[:].unsqueeze(2).to_broadcast([P, B, E]),
                                    ALU.subtract).then_inc(shift_ready, 1)
            dve.wait_ge(exp_ready, 1)
            after(nc.vector.reduce_sum(total[:], expo[:], AX_X))
            after(nc.vector.reciprocal(inv_total[:], total[:]))
            after(nc.vector.tensor_tensor(probs[:], expo[:], inv_total[:].unsqueeze(2).to_broadcast([P, B, E]),
                                          ALU.mult))
            for b in range(B):
                after(nc.vector.max(best[:, b], probs[:, b]))
                after(nc.vector.max_index(best_at[:, b], best[:, b], probs[:, b]))
            nc.vector.tensor_copy(chosen[0:1, :].rearrange("p (b k) -> p b k", b=B),
                                  best_at[0:1, :, 0:TOP_K]).then_inc(routed, 1)
            after(nc.vector.tensor_tensor(pair_sum[:], best[:, :, 0], best[:, :, 1], ALU.add))
            after(nc.vector.reciprocal(inv_pair[:], pair_sum[:]))
            after(nc.vector.tensor_tensor(norm_w[:], best[:, :, 0:TOP_K],
                                          inv_pair[:].unsqueeze(2).to_broadcast([P, B, TOP_K]), ALU.mult))
            after(nc.vector.tensor_scalar(scaled_w[:], norm_w[:], GRAD_SCALE, None, ALU.mult))
            dve.wait_ge(seg_one, 1)
            after(nc.vector.scalar_tensor_tensor(
                seg_w[:, 1:1 + B * TOP_K].rearrange("p (b k) -> p b k", b=B), norm_w[:], 1.0 - GRAD_SCALE,
                scaled_w[:], ALU.mult, ALU.add))

            def turn_half(b, half, job):
                dve.wait_ge(x_turned, job + 1)
                for kc, bank in enumerate((gate_ps[half], up_ps[half])):
                    at = x_cols(b, kc, half)
                    nc.vector.tensor_copy(x_t[:, at:at + HALF], bank[:]).then_inc(x_t_ready, 1)
                dve.wait_ge(x_hi_ready, KC * (job + 1))
                nc.vector.tensor_tensor(halves_view(x_lo, b, half), halves_view(x_t, b, half),
                                        halves_view(x_hi, b, half).bitcast(F32), ALU.subtract
                                        ).then_inc(x_split, 1)

            def unit_part(unit, k, s, pair):
                dve.wait_ge(gelu_ready, unit + 1)
                dve.wait_ge(up_ready, unit + 1)
                nc.vector.scalar_tensor_tensor(prod[:, k % 2], gelu[:, k % 2], seg_w[:, bass.ds(s, 1)],
                                               up_ps[pair][:], ALU.mult, ALU.mult).then_inc(prod_ready, 1)
                dve.wait_ge(h_hi_ready, unit + 1)
                nc.vector.tensor_tensor(h_lo[:, k % 2], prod[:, k % 2], h_hi[:, k % 2].bitcast(F32),
                                        ALU.subtract).then_inc(h_split, 1)

            def take_sum(s, b, half):
                dve.wait_ge(down_done, UNITS * s + UNITS - HALVES + half + 1)
                for m in range(KC):
                    at = bass.ds(b * BSTEP + m * S + half * HALF, HALF)
                    done = nc.vector.tensor_tensor(x_t[:, at], x_t[:, at], sum_ps[half][m][:], ALU.add)
                done.then_inc(sum_taken, 1)

            turn_half(0, 0, 0)
            turn_half(0, 1, 1)
            for k in range(UNITS_Q):
                unit_part(k, k, 0, k % 2)
            turn_half(1, 0, 2)
            turn_half(1, 1, 3)
            with dve.Fori(0, SEGMENTS - 1) as s:
                batch = dve.snap(s // SEG_PER_BATCH)
                for k in range(UNITS_Q, UNITS):
                    unit_part(UNITS * s + k, k, s, k % 2)
                take_sum(s, batch, 0)
                for k in range(UNITS_Q):
                    unit_part(UNITS * (s + 1) + k, k, s + 1, k % 2)
                    if k == 0:
                        take_sum(s, batch, 1)
            s = SEGMENTS - 1
            jobs = JOBS_BEFORE_LOOP + UNITS * (SEGMENTS - 1)
            for k in range(UNITS_Q, UNITS):
                if k == LIN_TURN_AT:
                    dve.wait_ge(lin_turned, 1)
                    wb_ps, lb_ps = gate_ps[jobs % 2], up_ps[jobs % 2]
                    nc.vector.tensor_copy(wb_t[:], wb_ps[:].rearrange("p (k n) -> p k n", k=KC)
                                          ).then_inc(wb_copied, 1)
                    for b in range(B):
                        nc.vector.tensor_scalar(lb_t[:, b], lb_ps[:, 0:H], lora_w[:, b:b + 1], LORA_SCALING,
                                                ALU.mult, ALU.mult).then_inc(wb_copied, 1)
                    dve.wait_ge(wb_copied, 1 + B)
                    for kc in range(KC):
                        block_kc = wb_t[:, kc, kc * P:(kc + 1) * P]
                        done = nc.vector.tensor_tensor(block_kc, block_kc, ident[:], ALU.add)
                    done.then_inc(lin_t_ready, 1)
                    jobs += 1
                if k == LIN_MIX_AT:
                    dve.wait_ge(lin_mixed, 1)
                    dve.wait_ge(lin_t_ready, 1)
                    for kc, bank in enumerate((gate_ps[jobs % 2], up_ps[jobs % 2])):
                        for b in range(B):
                            done = nc.vector.tensor_tensor(lin[:, b, kc], bank[:, b * H:(b + 1) * H],
                                                           wb_t[:, kc], ALU.add)
                    done.then_inc(lin_ready, 1)
                    jobs += 1
                unit_part(UNITS * s + k, k, s, jobs % 2)
                jobs += 1

            def out_half(b, half, n):
                for j, bank in enumerate((gate_ps[n % 2], up_ps[n % 2])):
                    dve.wait_ge(out_ps_ready, 2 * (n - jobs) + j + 1)
                    last = nc.vector.tensor_tensor(
                        x_rows[:, b, half, 2 * j:2 * j + 2], bank[:].rearrange("p (t n) -> p t n", t=2),
                        bias[:].unsqueeze(1).to_broadcast([P, 2, H]), ALU.add)
                    last.then_inc(out_ready, 1)

            def last_lo(half):
                dve.wait_ge(y_hi_ready, HALVES + half + 1)
                nc.vector.tensor_tensor(halves_view(x_lo, 1, half), halves_view(x_t, 1, half),
                                        halves_view(x_hi, 1, half).bitcast(F32), ALU.subtract
                                        ).then_inc(y_split_last, 1)

            take_sum(s, B - 1, 0)
            out_half(0, 0, jobs)
            take_sum(s, B - 1, 1)
            last_lo(0)
            last_lo(1)
            out_half(0, 1, jobs + 1)
            out_half(1, 0, jobs + 2)
            out_half(1, 1, jobs + 3)

        @block.tensor
        def _(pe):
            def turn_half(b, half, job):
                pe.wait_ge(x_in[b][half], 16)
                if job >= HALVES:
                    pe.wait_ge(prod_ready, UNITS_Q)
                for kc, bank in enumerate((gate_ps[half], up_ps[half])):
                    for t in range(TILES):
                        done = nc.tensor.transpose(bank[:, t * P:(t + 1) * P],
                                                   x_rows[:, b, half, t, kc * P:(kc + 1) * P], ident[:])
                done.then_inc(x_turned, 1)

            def gate_up(k, x_off, pair):
                q, c, half = unit_at(k)
                cols = slice(c * P, (c + 1) * P)
                for m, (bank, ready) in enumerate(((gate_ps[pair], gate_ready), (up_ps[pair], up_ready))):
                    passes = [(w, xs, kc) for kc in range(KC)
                              for w, xs in ((gu_hi, x_hi), (gu_hi, x_lo), (gu_lo, x_hi))]
                    for i, (w, xs, kc) in enumerate(passes):
                        rhs = xs[:, bass.ds(x_off + (kc * S + half * HALF), HALF)]
                        done = nc.tensor.matmul(bank[:], w[:, q, m, kc, cols], rhs,
                                                start=(i == 0), stop=(i == len(passes) - 1))
                    done.then_inc(ready, 1)

            def down(k):
                q, c, half = unit_at(k)
                first, last = k < HALVES, k >= UNITS - HALVES
                for m in range(KC):
                    cols = slice(m * P, (m + 1) * P)
                    passes = ((dn_hi, h_hi), (dn_hi, h_lo), (dn_lo, h_hi))
                    for i, (w, hs) in enumerate(passes):
                        done = nc.tensor.matmul(sum_ps[half][m][:], w[:, q, c, cols], hs[:, k % 2],
                                                start=(first and i == 0), stop=(last and i == 2))
                done.then_inc(down_done, 1)

            def unit_down(s, k):
                if k % UNITS_Q == 0:
                    pe.wait_ge(dn_split, QUARTERS * s + k // UNITS_Q + 1)
                if k < HALVES:
                    pe.wait_ge(sum_taken, HALVES * s + k - HALVES + 1)
                pe.wait_ge(h_split, UNITS * s + k + 1)
                down(k)

            pe.wait_ge(ident_ready, 1)
            turn_half(0, 0, 0)
            turn_half(0, 1, 1)
            pe.wait_ge(gu_split, 1)
            for k in range(UNITS_Q):
                if k < HALVES:
                    pe.wait_ge(x_split, k + 1)
                else:
                    pe.wait_ge(prod_ready, k - 1)
                gate_up(k, 0, k % 2)
                if k == 1:
                    pe.wait_ge(dn_split, 1)
                if k >= 1:
                    pe.wait_ge(h_split, k)
                    down(k - 1)
            turn_half(1, 0, 2)
            turn_half(1, 1, 3)
            pe.wait_ge(x_split, B * HALVES)

            def loop_unit(s, k, x_off):
                if k % UNITS_Q == 0:
                    pe.wait_ge(gu_split, QUARTERS * s + k // UNITS_Q + 1)
                pe.wait_ge(prod_ready, UNITS * s + k - 1)
                gate_up(k, x_off, k % 2)

            with pe.Fori(0, SEGMENTS - 1) as s:
                x_off = pe.snap((s // SEG_PER_BATCH) * BSTEP)
                for k in range(UNITS_Q, UNITS):
                    loop_unit(s, k, x_off)
                    if k == UNITS_Q:
                        pe.wait_ge(h_split, UNITS * s + k)
                        down(k - 1)
                    else:
                        unit_down(s, k - 1)
                x_next = pe.snap(((s + 1) // SEG_PER_BATCH) * BSTEP)
                for k in range(UNITS_Q):
                    loop_unit(s + 1, k, x_next)
                    if k == 0:
                        pe.wait_ge(h_split, UNITS * s + UNITS)
                        down(UNITS - 1)
                    else:
                        unit_down(s + 1, k - 1)

            s = SEGMENTS - 1
            jobs = JOBS_BEFORE_LOOP + UNITS * (SEGMENTS - 1)
            for k in range(UNITS_Q, UNITS):
                if k == LIN_TURN_AT:
                    pe.wait_ge(small_in, SMALL_LOADS * 16)
                    pe.wait_ge(prod_ready, UNITS * s + k - 1)
                    for kc in range(KC):
                        for oc in range(KC):
                            nc.tensor.transpose(gate_ps[jobs % 2][:, kc * H + oc * P:kc * H + (oc + 1) * P],
                                                wb_rows[:, oc, kc * P:(kc + 1) * P], ident[:])
                    for oc in range(KC):
                        done = nc.tensor.transpose(up_ps[jobs % 2][:, oc * P:(oc + 1) * P],
                                                   lb_rows[:, oc].rearrange("p e r -> p (e r)"), ident[:])
                    done.then_inc(lin_turned, 1)
                    jobs += 1
                if k == LIN_MIX_AT:
                    pe.wait_ge(lin_t_ready, 1)
                    for kc, bank in enumerate((gate_ps[jobs % 2], up_ps[jobs % 2])):
                        done = nc.tensor.matmul(bank[:], la_sb[:, kc * P:(kc + 1) * P],
                                                lb_t[:].rearrange("p b n -> p (b n)"), start=True, stop=True)
                    done.then_inc(lin_mixed, 1)
                    jobs += 1
                if k % UNITS_Q == 0:
                    pe.wait_ge(gu_split, QUARTERS * s + k // UNITS_Q + 1)
                if k in (LIN_TURN_AT, LIN_MIX_AT):
                    pe.wait_ge(prod_ready, UNITS * s + k)
                elif k == LIN_MIX_AT + 1:
                    pe.wait_ge(lin_ready, 1)
                else:
                    pe.wait_ge(prod_ready, UNITS * s + k - 1)
                gate_up(k, (B - 1) * BSTEP, jobs % 2)
                jobs += 1
                unit_down(s, k - 1)

            def second_layer(b, half, job):
                for j, bank in enumerate((gate_ps[job % 2], up_ps[job % 2])):
                    for t in (2 * j, 2 * j + 1):
                        passes = [(xs, w, kc) for kc in range(KC)
                                  for xs, w in ((x_hi, lin_hi), (x_hi, lin_lo), (x_lo, lin_hi))]
                        for i, (xs, w, kc) in enumerate(passes):
                            at = x_cols(b, kc, half) + t * P
                            done = nc.tensor.matmul(bank[:, (t % 2) * H:(t % 2 + 1) * H], xs[:, at:at + P],
                                                    w[:, b, kc], start=(i == 0), stop=(i == len(passes) - 1))
                    done.then_inc(out_ps_ready, 1)

            pe.wait_ge(lin_split, 1)
            pe.wait_ge(y_split, HALVES)
            pe.wait_ge(prod_ready, UNITS * SEGMENTS - 1)
            second_layer(0, 0, jobs)
            unit_down(s, UNITS - 1)
            pe.wait_ge(prod_ready, UNITS * SEGMENTS)
            second_layer(0, 1, jobs + 1)
            pe.wait_ge(out_ready, 2)
            pe.wait_ge(y_split_last, 1)
            second_layer(1, 0, jobs + 2)
            pe.wait_ge(y_split_last, 2)
            pe.wait_ge(out_ready, 4)
            second_layer(1, 1, jobs + 3)


_INS = ['x', 'cond_8', 'L0_cond_skill_gate', 'L0_cond_skill_up', 'L0_cond_skill_down',
        'L0_cond_shared_gate', 'L0_cond_shared_up', 'L0_cond_shared_down',
        'L1_cond_W_base', 'L1_cond_b_base', 'L1_cond_As', 'L1_cond_Bs']


def kernel(**inputs):
    import numpy as _np
    import concourse.bacc as _bacc
    from concourse import mybir as _mybir
    from concourse.bass_utils import run_bass_kernel_spmd as _run

    nc = _bacc.Bacc("TRN2", target_bir_lowering=False, num_devices=1)
    arrays, args = {}, []
    for name in _INS:
        a = _np.ascontiguousarray(inputs[name])
        arrays[f"in_{name}"] = a
        args.append(nc.dram_tensor(f"in_{name}", a.shape, _mybir.dt.from_np(a.dtype), kind="ExternalInput").ap())
    shape = arrays["in_x"].shape
    args.append(nc.dram_tensor("out_0", shape, _mybir.dt.float32, kind="ExternalOutput").ap())
    moe_lora_program(nc, *args)
    r = _run(nc, [arrays], core_ids=[0])
    return r.results[0]["out_0"]
```

```python
import concourse.bass as bass
from concourse import mybir
from contextlib import ExitStack


def moe_lora_program(nc, x, cond, skill_gate, skill_up, skill_down, shared_gate, shared_up,
                     shared_down, w_base, b_base, lora_a, lora_b, out):
    F32 = mybir.dt.float32
    F32R = mybir.dt.float32r
    U32 = mybir.dt.uint32
    ALU = mybir.AluOpType
    ACT = mybir.ActivationFunctionType
    AX_X = mybir.AxisListType.X

    P = 128
    B, S, H = x.shape
    E, _, I = skill_gate.shape
    R = lora_a.shape[1]
    KC = H // P
    HALF = 512
    HALVES = S // HALF
    TILES = HALF // P
    QUARTERS = 4
    IQ = I // QUARTERS
    CQ = IQ // P
    TOP_K = 2
    NUM_MOE_LAYERS = 12
    GRAD_SCALE = 1.0 / NUM_MOE_LAYERS
    LORA_SCALING = 32.0 / R
    SEGMENTS = B * (TOP_K + 1)
    SEG_PER_BATCH = TOP_K + 1
    UNITS_Q = CQ * HALVES
    UNITS = QUARTERS * UNITS_Q
    BSTEP = KC * S
    JOBS_BEFORE_LOOP = B * HALVES + UNITS_Q
    WARM_UP = 6
    LAG = 2
    H_BUFS = 4
    SPLIT_AT = 2
    TURN_AFTER = 2
    LIN_TURN_AT = 2 * UNITS_Q
    LIN_MIX_AT = LIN_TURN_AT + 1
    SMALL_LOADS = 1 + KC + 2

    ctx = ExitStack()
    with ctx:
        def sb(name, shape, dt=F32):
            return ctx.enter_context(nc.sbuf_tensor(name, shape, dt))

        def sem(name):
            return ctx.enter_context(nc.semaphore(name))

        x_rows = sb("x_rows", [P, B, HALVES, TILES, H])
        x_t = sb("x_t", [P, B * KC * S])
        x_hi = sb("x_hi", [P, B * KC * S], F32R)
        x_lo = sb("x_lo", [P, B * KC * S], F32R)
        gu_stage = sb("gu_stage", [P, QUARTERS, 2, KC, IQ])
        dn_stage = sb("dn_stage", [P, QUARTERS, CQ, H])
        gu_hi = sb("gu_hi", [P, QUARTERS, 2, KC, IQ], F32R)
        gu_lo = sb("gu_lo", [P, QUARTERS, 2, KC, IQ], F32R)
        dn_hi = sb("dn_hi", [P, QUARTERS, CQ, H], F32R)
        dn_lo = sb("dn_lo", [P, QUARTERS, CQ, H], F32R)
        gelu = sb("gelu", [P, 2, HALF])
        prod = sb("prod", [P, 2, HALF])
        h_hi = sb("h_hi", [P, H_BUFS, HALF], F32R)
        h_lo = sb("h_lo", [P, H_BUFS, HALF], F32R)
        ident = sb("ident", [P, P])
        wb_rows = sb("wb_rows", [P, KC, H])
        lb_rows = sb("lb_rows", [P, KC, E, R])
        la_sb = sb("la_sb", [P, H])
        bias = sb("bias", [P, H])
        lora_w = sb("lora_w", [P, B])
        wb_t = sb("wb_t", [P, KC, H])
        lb_t = sb("lb_t", [P, B, H])
        lin = sb("lin", [P, B, KC, H])
        lin_hi = sb("lin_hi", [P, B, KC, H], F32R)
        lin_lo = sb("lin_lo", [P, B, KC, H], F32R)
        own_expert = sb("own_expert", [P, E])
        own_logits = sb("own_logits", [P, B, E])
        logits = sb("logits", [P, B, E])
        top = sb("top", [P, B])
        shifted = sb("shifted", [P, B, E])
        table_probe = sb("table_probe", [P, 1])
        expo = sb("expo", [P, B, E])
        total = sb("total", [P, B])
        inv_total = sb("inv_total", [P, B])
        probs = sb("probs", [P, B, E])
        best = sb("best", [P, B, 8])
        best_at = sb("best_at", [P, B, 8], U32)
        pair_sum = sb("pair_sum", [P, B])
        inv_pair = sb("inv_pair", [P, B])
        norm_w = sb("norm_w", [P, B, TOP_K])
        scaled_w = sb("scaled_w", [P, B, TOP_K])
        seg_w = sb("seg_w", [P, SEGMENTS])
        chosen = sb("chosen", [1, B * TOP_K], U32)

        gate_ps = [ctx.enter_context(nc.psum_tensor(f"gate_ps{i}", [P, HALF], F32)) for i in range(2)]
        up_ps = [ctx.enter_context(nc.psum_tensor(f"up_ps{i}", [P, HALF], F32)) for i in range(2)]
        sum_ps = [[ctx.enter_context(nc.psum_tensor(f"sum_ps{h}{m}", [P, HALF], F32))
                   for m in range(KC)] for h in range(HALVES)]

        x_in = [[sem(f"x_in{b}{h}") for h in range(HALVES)] for b in range(B)]
        gu_in = [[sem(f"{m}_in{q}") for q in range(QUARTERS)]
                 for m in ("gate", "up")]
        dn_in = [sem(f"dn_in{q}") for q in range(QUARTERS)]
        logits_in = sem("logits_in")
        own_step = sem("own_step")
        small_in = sem("small_in")
        seg_one = sem("seg_one")
        ident_zero = sem("ident_zero")
        ident_ready = sem("ident_ready")
        route_step = sem("route_step")
        shift_ready = sem("shift_ready")
        exp_ready = sem("exp_ready")
        routed = sem("routed")
        x_turned = sem("x_turned")
        x_hi_ready = sem("x_hi_ready")
        x_t_ready = sem("x_t_ready")
        x_split = sem("x_split")
        gu_hi_ready = sem("gu_hi_ready")
        gu_split = sem("gu_split")
        dn_hi_ready = sem("dn_hi_ready")
        dn_split = sem("dn_split")
        gate_ready = sem("gate_ready")
        up_ready = sem("up_ready")
        gelu_ready = sem("gelu_ready")
        prod_ready = sem("prod_ready")
        h_hi_ready = sem("h_hi_ready")
        h_split = sem("h_split")
        down_done = sem("down_done")
        sum_taken = sem("sum_taken")
        lin_turned = sem("lin_turned")
        wb_copied = sem("wb_copied")
        lin_t_ready = sem("lin_t_ready")
        lin_mixed = sem("lin_mixed")
        lin_ready = sem("lin_ready")
        lin_hi_ready = sem("lin_hi_ready")
        lin_split = sem("lin_split")
        y_hi_ready = sem("y_hi_ready")
        y_split = sem("y_split")
        y_split_last = sem("y_split_last")
        out_ps_ready = sem("out_ps_ready")
        out_ready = sem("out_ready")
        out_stored = sem("out_stored")

        def unit_at(k):
            return k // UNITS_Q, k % UNITS_Q // HALVES, k % HALVES

        def x_cols(b, kc, half):
            return b * BSTEP + kc * S + half * HALF

        def turn_banks(half, job):
            pair = (half + job // HALVES) % 2
            return gate_ps[pair], up_ps[pair]

        def halves_view(tile, b, half):
            return tile[:, b * BSTEP:(b + 1) * BSTEP].rearrange("p (k s) -> p k s", k=KC)[
                :, :, half * HALF:(half + 1) * HALF]

        x_dram = x.rearrange("b (h p t) c -> b h p t c", h=HALVES, t=TILES)
        out_dram = out.rearrange("b (h p t) c -> b h p t c", h=HALVES, t=TILES)

        block = ctx.enter_context(nc.Block())

        @block.sync
        def _(sp):
            def load_x(b, half):
                sp.dma_start(x_rows[:, b, half], x_dram[b, half]).then_inc(x_in[b][half], 16)

            def load_gate_up(m, w, slot):
                cols = slice(slot * IQ, (slot + 1) * IQ)
                sp.dma_start(gu_stage[:, slot, m],
                             w[:, cols].rearrange("(k p) n -> p k n", p=P)).then_inc(gu_in[m][slot], 16)

            def load_down(w, slot):
                rows = slice(slot * IQ, (slot + 1) * IQ)
                sp.dma_start(dn_stage[:, slot],
                             w[rows, :].rearrange("(c p) n -> p c n", p=P)).then_inc(dn_in[slot], 16)

            def load_quarter(gate, up, down, slot):
                load_gate_up(0, gate, slot)
                load_gate_up(1, up, slot)
                load_down(down, slot)

            sp.dma_start(logits[:], cond.partition_broadcast(P)).then_inc(logits_in, 16)
            load_x(0, 0)
            load_gate_up(0, shared_gate, 0)
            load_x(0, 1)
            load_gate_up(1, shared_up, 0)
            load_down(shared_down, 0)
            load_x(1, 0)
            load_x(1, 1)
            for q in range(1, QUARTERS):
                load_quarter(shared_gate, shared_up, shared_down, q)
            sp.dma_start(wb_rows[:], w_base.rearrange("(k p) c -> p k c", p=P)).then_inc(small_in, 16)
            for k in range(KC):
                sp.dma_start(lb_rows[:, k], lora_b[:, k * P:(k + 1) * P, :].rearrange("e p r -> p e r")
                             ).then_inc(small_in, 16)
            sp.dma_start(la_sb[:], lora_a.rearrange("e r c -> (e r) c")).then_inc(small_in, 16)
            sp.dma_start(bias[:], b_base.partition_broadcast(P)).then_inc(small_in, 16)
            sp.wait_ge(routed, 1)
            with sp.Fori(1, SEGMENTS - 1) as s:
                e = sp.value_load(chosen[0:1, bass.ds(s - 1, 1)], min_val=0, max_val=E - 1)
                for q in range(QUARTERS):
                    sp.wait_ge(dn_split, QUARTERS * s + q - QUARTERS + 1)
                    gate = skill_gate[bass.ds(e, 1)].rearrange("e h i -> (e h) i")
                    up = skill_up[bass.ds(e, 1)].rearrange("e h i -> (e h) i")
                    down = skill_down[bass.ds(e, 1)].rearrange("e i h -> (e i) h")
                    load_quarter(gate, up, down, q)
            for q in range(QUARTERS):
                done = QUARTERS * (SEGMENTS - 2) + q + 1
                sp.wait_ge(dn_split, done)
                load_quarter(shared_gate, shared_up, shared_down, q)
            stored = 0
            for b in range(B):
                for half in range(HALVES):
                    for j in range(TILES // 2):
                        stored += 1
                        sp.wait_ge(out_ready, stored)
                        sp.dma_start(out_dram[b, half, :, 2 * j:2 * j + 2],
                                     x_rows[:, b, half, 2 * j:2 * j + 2]).then_inc(out_stored, 16)
            sp.wait_ge(out_stored, 16 * stored)

        @block.gpsimd
        def _(pool):
            nc.gpsimd.memset(ident[:], 0.0).then_inc(ident_zero, 1)
            nc.gpsimd.memset(seg_w[:], 1.0).then_inc(seg_one, 1)
            pool.wait_ge(ident_zero, 1)
            nc.gpsimd.affine_select(out=ident[:], in_=ident[:], compare_op=ALU.not_equal, fill=1.0,
                                    base=0, pattern=[[-1, P]], channel_multiplier=1
                                    ).then_inc(ident_ready, 1)
            nc.gpsimd.memset(own_expert[:], 1.0).then_inc(own_step, 1)
            pool.wait_ge(own_step, 1)
            nc.gpsimd.affine_select(out=own_expert[:], in_=own_expert[:], compare_op=ALU.is_ge, fill=0.0,
                                    base=0, pattern=[[-R, E]], channel_multiplier=1).then_inc(own_step, 1)
            pool.wait_ge(own_step, 2)
            nc.gpsimd.affine_select(out=own_expert[:], in_=own_expert[:], compare_op=ALU.is_ge, fill=0.0,
                                    base=R - 1, pattern=[[R, E]], channel_multiplier=-1).then_inc(own_step, 1)

            def lo_part(n, slot):
                for m in range(2):
                    pool.wait_ge(gu_hi_ready, 2 * n + m + 1)
                    nc.gpsimd.tensor_tensor(gu_lo[:, slot, m], gu_stage[:, slot, m],
                                            gu_hi[:, slot, m].bitcast(F32), ALU.subtract).then_inc(gu_split, 1)
                pool.wait_ge(dn_hi_ready, n + 1)
                nc.gpsimd.tensor_tensor(dn_lo[:, slot], dn_stage[:, slot], dn_hi[:, slot].bitcast(F32),
                                        ALU.subtract).then_inc(dn_split, 1)

            for n in range(QUARTERS):
                lo_part(n, n)
            with pool.Fori(1, SEGMENTS) as s:
                for q in range(QUARTERS):
                    lo_part(QUARTERS * s + q, q)
            for half in range(HALVES):
                pool.wait_ge(y_hi_ready, half + 1)
                nc.gpsimd.tensor_tensor(halves_view(x_lo, 0, half), halves_view(x_t, 0, half),
                                        halves_view(x_hi, 0, half).bitcast(F32), ALU.subtract
                                        ).then_inc(y_split, 1)
            pool.wait_ge(lin_hi_ready, 1)
            nc.gpsimd.tensor_tensor(lin_lo[:], lin[:], lin_hi[:].bitcast(F32), ALU.subtract
                                    ).then_inc(lin_split, 1)

        @block.scalar
        def _(act):
            act.wait_ge(shift_ready, 1)
            nc.scalar.activation(expo[:], shifted[:], ACT.Exp).then_inc(exp_ready, 1)
            nc.scalar.activation(table_probe[:], shifted[:, 0, 0:1], ACT.Gelu_apprx_tanh)

            def x_hi_part(b, half, job):
                for kc in range(KC):
                    act.wait_ge(x_t_ready, KC * job + kc + 1)
                    at = x_cols(b, kc, half)
                    nc.scalar.activation(x_hi[:, at:at + HALF], x_t[:, at:at + HALF], ACT.Copy
                                         ).then_inc(x_hi_ready, 1)

            def one_hi_part(m, slot, fill):
                act.wait_ge(gu_in[m][slot], 16 * fill)
                nc.scalar.activation(gu_hi[:, slot, m], gu_stage[:, slot, m], ACT.Copy
                                     ).then_inc(gu_hi_ready, 1)

            def gu_hi_part(slot, fill):
                one_hi_part(0, slot, fill)
                one_hi_part(1, slot, fill)

            def dn_hi_part(slot, fill):
                act.wait_ge(dn_in[slot], 16 * fill)
                nc.scalar.activation(dn_hi[:, slot], dn_stage[:, slot], ACT.Copy).then_inc(dn_hi_ready, 1)

            def gelu_part(unit, k):
                act.wait_ge(gate_ready, unit + 1)
                nc.scalar.activation(gelu[:, k % 2], gate_ps[k % 2][:], ACT.Gelu_apprx_tanh
                                     ).then_inc(gelu_ready, 1)

            def h_hi_part(unit, k):
                act.wait_ge(prod_ready, unit + 1)
                nc.scalar.activation(h_hi[:, k % H_BUFS], prod[:, k % 2], ACT.Copy).then_inc(h_hi_ready, 1)

            one_hi_part(0, 0, 1)
            x_hi_part(0, 0, 0)
            one_hi_part(1, 0, 1)
            x_hi_part(0, 1, 1)
            dn_hi_part(0, 1)
            for k in range(UNITS_Q):
                gelu_part(k, k)
                h_hi_part(k, k)
                if k in (0, TURN_AFTER):
                    gu_hi_part(1 + k // TURN_AFTER, 1)
                    dn_hi_part(1 + k // TURN_AFTER, 1)
            x_hi_part(1, 0, 2)
            x_hi_part(1, 1, 3)
            gu_hi_part(3, 1)
            dn_hi_part(3, 1)
            with act.Fori(0, SEGMENTS - 1) as s:
                for q in range(1, QUARTERS):
                    for j in range(UNITS_Q):
                        k = q * UNITS_Q + j
                        gelu_part(UNITS * s + k, k)
                        h_hi_part(UNITS * s + k, k)
                        if j == SPLIT_AT:
                            act.wait_ge(down_done, UNITS * s + q * UNITS_Q)
                            gu_hi_part(q - 1, s + 2)
                        if j == SPLIT_AT + 1:
                            dn_hi_part(q - 1, s + 2)
                for k in range(UNITS_Q):
                    gelu_part(UNITS * (s + 1) + k, k)
                    h_hi_part(UNITS * (s + 1) + k, k)
                    if k == SPLIT_AT:
                        act.wait_ge(down_done, UNITS * (s + 1))
                        gu_hi_part(QUARTERS - 1, s + 2)
                    if k == SPLIT_AT + 1:
                        dn_hi_part(QUARTERS - 1, s + 2)
            s = SEGMENTS - 1
            jobs = JOBS_BEFORE_LOOP + UNITS * (SEGMENTS - 1)
            for k in range(UNITS_Q, UNITS):
                if k == LIN_TURN_AT or k == LIN_MIX_AT:
                    jobs += 1
                act.wait_ge(gate_ready, UNITS * s + k + 1)
                nc.scalar.activation(gelu[:, k % 2], gate_ps[jobs % 2][:], ACT.Gelu_apprx_tanh
                                     ).then_inc(gelu_ready, 1)
                jobs += 1
                h_hi_part(UNITS * s + k, k)
                if k in (UNITS_Q, UNITS_Q + 1):
                    half = k - UNITS_Q
                    act.wait_ge(sum_taken, HALVES * SEG_PER_BATCH)
                    nc.scalar.activation(halves_view(x_hi, 0, half), halves_view(x_t, 0, half), ACT.Copy
                                         ).then_inc(y_hi_ready, 1)
                if k == LIN_MIX_AT + 1:
                    act.wait_ge(lin_ready, 1)
                    nc.scalar.activation(lin_hi[:], lin[:], ACT.Copy).then_inc(lin_hi_ready, 1)
            for half in range(HALVES):
                act.wait_ge(sum_taken, HALVES * (SEGMENTS - 1) + half + 1)
                nc.scalar.activation(halves_view(x_hi, 1, half), halves_view(x_t, 1, half), ACT.Copy
                                     ).then_inc(y_hi_ready, 1)

        @block.vector
        def _(dve):
            steps = [0]

            def after(instruction):
                steps[0] += 1
                instruction.then_inc(route_step, 1)
                dve.wait_ge(route_step, steps[0])

            def route():
                dve.wait_ge(logits_in, 16)
                after(nc.vector.reduce_max(top[:], logits[:], AX_X))
                nc.vector.tensor_tensor(shifted[:], logits[:], top[:].unsqueeze(2).to_broadcast([P, B, E]),
                                        ALU.subtract).then_inc(shift_ready, 1)
                dve.wait_ge(exp_ready, 1)
                after(nc.vector.reduce_sum(total[:], expo[:], AX_X))
                after(nc.vector.reciprocal(inv_total[:], total[:]))
                after(nc.vector.tensor_tensor(probs[:], expo[:], inv_total[:].unsqueeze(2).to_broadcast([P, B, E]),
                                              ALU.mult))
                for b in range(B):
                    after(nc.vector.max(best[:, b], probs[:, b]))
                    after(nc.vector.max_index(best_at[:, b], best[:, b], probs[:, b]))
                nc.vector.tensor_copy(chosen[0:1, :].rearrange("p (b k) -> p b k", b=B),
                                      best_at[0:1, :, 0:TOP_K]).then_inc(routed, 1)

            def weigh():
                after(nc.vector.tensor_tensor(pair_sum[:], best[:, :, 0], best[:, :, 1], ALU.add))
                after(nc.vector.reciprocal(inv_pair[:], pair_sum[:]))
                after(nc.vector.tensor_tensor(norm_w[:], best[:, :, 0:TOP_K],
                                              inv_pair[:].unsqueeze(2).to_broadcast([P, B, TOP_K]), ALU.mult))
                after(nc.vector.tensor_scalar(scaled_w[:], norm_w[:], GRAD_SCALE, None, ALU.mult))
                after(nc.vector.scalar_tensor_tensor(
                    seg_w[:, 1:1 + B * TOP_K].rearrange("p (b k) -> p b k", b=B), norm_w[:], 1.0 - GRAD_SCALE,
                    scaled_w[:], ALU.mult, ALU.add))

                dve.wait_ge(own_step, 3)
                after(nc.vector.tensor_tensor(own_logits[:], logits[:],
                                              own_expert[:].unsqueeze(1).to_broadcast([P, B, E]), ALU.mult))
                after(nc.vector.reduce_sum(lora_w[:], own_logits[:], AX_X))

            def copy_half(b, half, job):
                for kc, bank in enumerate(turn_banks(half, job)):
                    dve.wait_ge(x_turned, KC * job + kc + 1)
                    at = x_cols(b, kc, half)
                    nc.vector.tensor_copy(x_t[:, at:at + HALF], bank[:]).then_inc(x_t_ready, 1)

            def lo_half(b, half, job):
                for kc in range(KC):
                    dve.wait_ge(x_hi_ready, KC * job + kc + 1)
                    at = x_cols(b, kc, half)
                    nc.vector.tensor_tensor(x_lo[:, at:at + HALF], x_t[:, at:at + HALF],
                                            x_hi[:, at:at + HALF].bitcast(F32), ALU.subtract
                                            ).then_inc(x_split, 1)

            def prod_part(unit, k, s, pair):
                dve.wait_ge(gelu_ready, unit + 1)
                dve.wait_ge(up_ready, unit + 1)
                nc.vector.scalar_tensor_tensor(prod[:, k % 2], gelu[:, k % 2], seg_w[:, bass.ds(s, 1)],
                                               up_ps[pair][:], ALU.mult, ALU.mult).then_inc(prod_ready, 1)

            def h_lo_part(unit, k):
                dve.wait_ge(h_hi_ready, unit + 1)
                nc.vector.tensor_tensor(h_lo[:, k % H_BUFS], prod[:, k % 2], h_hi[:, k % H_BUFS].bitcast(F32),
                                        ALU.subtract).then_inc(h_split, 1)

            def unit_part(unit, k, s, pair):
                prod_part(unit, k, s, pair)
                h_lo_part(unit, k)

            def take_sum(s, b, half):
                dve.wait_ge(down_done, UNITS * s + UNITS - HALVES + half + 1)
                for m in range(KC):
                    at = bass.ds(b * BSTEP + m * S + half * HALF, HALF)
                    done = nc.vector.tensor_tensor(x_t[:, at], x_t[:, at], sum_ps[half][m][:], ALU.add)
                done.then_inc(sum_taken, 1)

            route()
            copy_half(0, 0, 0)
            lo_half(0, 0, 0)
            copy_half(0, 1, 1)
            lo_half(0, 1, 1)
            dve.wait_ge(seg_one, 1)
            for k in range(UNITS_Q):
                prod_part(k, k, 0, k % 2)
                if k == TURN_AFTER:
                    copy_half(1, 0, 2)
                h_lo_part(k, k)
                if k == 0:
                    weigh()
                if k == TURN_AFTER:
                    copy_half(1, 1, 3)
            lo_half(1, 0, 2)
            lo_half(1, 1, 3)
            with dve.Fori(0, SEGMENTS - 1) as s:
                batch = dve.snap(s // SEG_PER_BATCH)
                for k in range(UNITS_Q, UNITS):
                    unit_part(UNITS * s + k, k, s, k % 2)
                for k in range(UNITS_Q):
                    unit_part(UNITS * (s + 1) + k, k, s + 1, k % 2)
                    if k < HALVES:
                        take_sum(s, batch, k)
            s = SEGMENTS - 1
            jobs = JOBS_BEFORE_LOOP + UNITS * (SEGMENTS - 1)
            for k in range(UNITS_Q, UNITS):
                if k == LIN_TURN_AT:
                    dve.wait_ge(lin_turned, 1)
                    wb_ps, lb_ps = gate_ps[jobs % 2], up_ps[jobs % 2]
                    nc.vector.tensor_copy(wb_t[:], wb_ps[:].rearrange("p (k n) -> p k n", k=KC)
                                          ).then_inc(wb_copied, 1)
                    for b in range(B):
                        nc.vector.tensor_scalar(lb_t[:, b], lb_ps[:, 0:H], lora_w[:, b:b + 1], LORA_SCALING,
                                                ALU.mult, ALU.mult).then_inc(wb_copied, 1)
                    dve.wait_ge(wb_copied, 1 + B)
                    for kc in range(KC):
                        block_kc = wb_t[:, kc, kc * P:(kc + 1) * P]
                        done = nc.vector.tensor_tensor(block_kc, block_kc, ident[:], ALU.add)
                    done.then_inc(lin_t_ready, 1)
                    jobs += 1
                if k == LIN_MIX_AT:
                    dve.wait_ge(lin_mixed, 1)
                    dve.wait_ge(lin_t_ready, 1)
                    for kc, bank in enumerate((gate_ps[jobs % 2], up_ps[jobs % 2])):
                        for b in range(B):
                            done = nc.vector.tensor_tensor(lin[:, b, kc], bank[:, b * H:(b + 1) * H],
                                                           wb_t[:, kc], ALU.add)
                    done.then_inc(lin_ready, 1)
                    jobs += 1
                unit_part(UNITS * s + k, k, s, jobs % 2)
                jobs += 1

            def out_half(b, half, n):
                for j, bank in enumerate((gate_ps[n % 2], up_ps[n % 2])):
                    dve.wait_ge(out_ps_ready, 2 * (n - jobs) + j + 1)
                    last = nc.vector.tensor_tensor(
                        x_rows[:, b, half, 2 * j:2 * j + 2], bank[:].rearrange("p (t n) -> p t n", t=2),
                        bias[:].unsqueeze(1).to_broadcast([P, 2, H]), ALU.add)
                    last.then_inc(out_ready, 1)

            def last_lo(half):
                dve.wait_ge(y_hi_ready, HALVES + half + 1)
                nc.vector.tensor_tensor(halves_view(x_lo, 1, half), halves_view(x_t, 1, half),
                                        halves_view(x_hi, 1, half).bitcast(F32), ALU.subtract
                                        ).then_inc(y_split_last, 1)

            take_sum(s, B - 1, 0)
            take_sum(s, B - 1, 1)
            last_lo(0)
            out_half(0, 0, jobs)
            last_lo(1)
            out_half(0, 1, jobs + 1)
            out_half(1, 0, jobs + 2)
            out_half(1, 1, jobs + 3)

        @block.tensor
        def _(pe):
            def turn_half(b, half, job):
                pe.wait_ge(x_in[b][half], 16)
                if job >= HALVES:
                    pe.wait_ge(prod_ready, TURN_AFTER + half)
                for kc, bank in enumerate(turn_banks(half, job)):
                    for t in range(TILES):
                        done = nc.tensor.transpose(bank[:, t * P:(t + 1) * P],
                                                   x_rows[:, b, half, t, kc * P:(kc + 1) * P], ident[:])
                    done.then_inc(x_turned, 1)

            def gate_up(k, x_off, pair, s, x_new=False, copied=None):
                q, c, half = unit_at(k)
                cols = slice(c * P, (c + 1) * P)
                for m, (bank, ready) in enumerate(((gate_ps[pair], gate_ready), (up_ps[pair], up_ready))):
                    if copied is not None:
                        pe.wait_ge(x_t_ready, copied + m + 1)
                    if k % UNITS_Q == 0 and not x_new:
                        pe.wait_ge(gu_split, 2 * (QUARTERS * s + q) + m + 1)
                    passes = [(w, xs, kc) for w, xs in ((gu_hi, x_hi), (gu_lo, x_hi), (gu_hi, x_lo))
                              for kc in range(KC)]
                    for i, (w, xs, kc) in enumerate(passes):
                        if x_new and k == 0 and i == 0:
                            pe.wait_ge(gu_hi_ready, m + 1)
                        if x_new and k == 0 and i == KC:
                            pe.wait_ge(gu_split, m + 1)
                        if x_new and m == 0 and xs is x_hi and w is gu_hi:
                            pe.wait_ge(x_hi_ready, KC * half + kc + 1)
                        if x_new and m == 0 and xs is x_lo:
                            pe.wait_ge(x_split, KC * half + kc + 1)
                        rhs = xs[:, bass.ds(x_off + (kc * S + half * HALF), HALF)]
                        done = nc.tensor.matmul(bank[:], w[:, q, m, kc, cols], rhs,
                                                start=(i == 0), stop=(i == len(passes) - 1))
                    done.then_inc(ready, 1)

            def down(k):
                q, c, half = unit_at(k)
                first, last = k < HALVES, k >= UNITS - HALVES
                for m in range(KC):
                    cols = slice(m * P, (m + 1) * P)
                    passes = ((dn_hi, h_hi), (dn_hi, h_lo), (dn_lo, h_hi))
                    for i, (w, hs) in enumerate(passes):
                        done = nc.tensor.matmul(sum_ps[half][m][:], w[:, q, c, cols], hs[:, k % H_BUFS],
                                                start=(first and i == 0), stop=(last and i == 2))
                done.then_inc(down_done, 1)

            def unit_down(s, k):
                if k % UNITS_Q == 0:
                    pe.wait_ge(dn_split, QUARTERS * s + k // UNITS_Q + 1)
                if k < HALVES:
                    pe.wait_ge(sum_taken, HALVES * s + k - HALVES + 1)
                pe.wait_ge(h_split, UNITS * s + k + 1)
                down(k)

            pe.wait_ge(ident_ready, 1)
            for _ in range(WARM_UP):
                nc.tensor.matmul(sum_ps[HALVES - 1][KC - 1][:, 0:P], ident[:], ident[:], start=True, stop=True)
            turn_half(0, 0, 0)
            turn_half(0, 1, 1)
            for k in range(UNITS_Q):
                if k < HALVES:
                    gate_up(k, 0, k % 2, 0, x_new=True, copied=KC * k)
                elif k == TURN_AFTER + 1:
                    gate_up(k, 0, k % 2, 0, copied=KC * HALVES)
                else:
                    pe.wait_ge(prod_ready, k - 1)
                    gate_up(k, 0, k % 2, 0)
                if k == LAG:
                    pe.wait_ge(dn_split, 1)
                if k >= LAG:
                    pe.wait_ge(h_split, k - LAG + 1)
                    down(k - LAG)
                if k == TURN_AFTER:
                    turn_half(1, 0, 2)
                    turn_half(1, 1, 3)
            pe.wait_ge(x_t_ready, KC * B * HALVES)

            def loop_unit(s, k, x_off):
                pe.wait_ge(prod_ready, UNITS * s + k - 1)
                gate_up(k, x_off, k % 2, s)

            with pe.Fori(0, SEGMENTS - 1) as s:
                x_off = pe.snap((s // SEG_PER_BATCH) * BSTEP)
                for k in range(UNITS_Q, UNITS):
                    loop_unit(s, k, x_off)
                    unit_down(s, k - LAG)
                pe.wait_ge(x_split, KC * B * HALVES)
                x_next = pe.snap(((s + 1) // SEG_PER_BATCH) * BSTEP)
                for k in range(UNITS_Q):
                    loop_unit(s + 1, k, x_next)
                    if k < LAG:
                        unit_down(s, UNITS + k - LAG)
                    else:
                        unit_down(s + 1, k - LAG)

            s = SEGMENTS - 1
            jobs = JOBS_BEFORE_LOOP + UNITS * (SEGMENTS - 1)
            for k in range(UNITS_Q, UNITS):
                if k == LIN_TURN_AT:
                    pe.wait_ge(small_in, SMALL_LOADS * 16)
                    pe.wait_ge(prod_ready, UNITS * s + k - 1)
                    for kc in range(KC):
                        for oc in range(KC):
                            nc.tensor.transpose(gate_ps[jobs % 2][:, kc * H + oc * P:kc * H + (oc + 1) * P],
                                                wb_rows[:, oc, kc * P:(kc + 1) * P], ident[:])
                    for oc in range(KC):
                        done = nc.tensor.transpose(up_ps[jobs % 2][:, oc * P:(oc + 1) * P],
                                                   lb_rows[:, oc].rearrange("p e r -> p (e r)"), ident[:])
                    done.then_inc(lin_turned, 1)
                    jobs += 1
                if k == LIN_MIX_AT:
                    pe.wait_ge(lin_t_ready, 1)
                    for kc, bank in enumerate((gate_ps[jobs % 2], up_ps[jobs % 2])):
                        done = nc.tensor.matmul(bank[:], la_sb[:, kc * P:(kc + 1) * P],
                                                lb_t[:].rearrange("p b n -> p (b n)"), start=True, stop=True)
                    done.then_inc(lin_mixed, 1)
                    jobs += 1
                if k in (LIN_TURN_AT, LIN_MIX_AT):
                    pe.wait_ge(prod_ready, UNITS * s + k)
                elif k == LIN_MIX_AT + 1:
                    pe.wait_ge(lin_ready, 1)
                else:
                    pe.wait_ge(prod_ready, UNITS * s + k - 1)
                gate_up(k, (B - 1) * BSTEP, jobs % 2, s)
                jobs += 1
                unit_down(s, k - LAG)

            def second_layer(b, half, job):
                for j, bank in enumerate((gate_ps[job % 2], up_ps[job % 2])):
                    for t in (2 * j, 2 * j + 1):
                        passes = [(xs, w, kc) for kc in range(KC)
                                  for xs, w in ((x_hi, lin_hi), (x_hi, lin_lo), (x_lo, lin_hi))]
                        for i, (xs, w, kc) in enumerate(passes):
                            at = x_cols(b, kc, half) + t * P
                            done = nc.tensor.matmul(bank[:, (t % 2) * H:(t % 2 + 1) * H], xs[:, at:at + P],
                                                    w[:, b, kc], start=(i == 0), stop=(i == len(passes) - 1))
                    done.then_inc(out_ps_ready, 1)

            for k in range(UNITS - LAG, UNITS):
                unit_down(s, k)
            pe.wait_ge(lin_split, 1)
            pe.wait_ge(y_split, HALVES)
            pe.wait_ge(prod_ready, UNITS * SEGMENTS - 1)
            second_layer(0, 0, jobs)
            pe.wait_ge(prod_ready, UNITS * SEGMENTS)
            second_layer(0, 1, jobs + 1)
            pe.wait_ge(out_ready, 2)
            pe.wait_ge(y_split_last, 1)
            second_layer(1, 0, jobs + 2)
            pe.wait_ge(out_ready, 4)
            pe.wait_ge(y_split_last, 2)
            second_layer(1, 1, jobs + 3)


_INS = ['x', 'cond_8', 'L0_cond_skill_gate', 'L0_cond_skill_up', 'L0_cond_skill_down',
        'L0_cond_shared_gate', 'L0_cond_shared_up', 'L0_cond_shared_down',
        'L1_cond_W_base', 'L1_cond_b_base', 'L1_cond_As', 'L1_cond_Bs']


def kernel(**inputs):
    import numpy as _np
    import concourse.bacc as _bacc
    from concourse import mybir as _mybir
    from concourse.bass_utils import run_bass_kernel_spmd as _run

    nc = _bacc.Bacc("TRN2", target_bir_lowering=False, num_devices=1)
    arrays, args = {}, []
    for name in _INS:
        a = _np.ascontiguousarray(inputs[name])
        arrays[f"in_{name}"] = a
        args.append(nc.dram_tensor(f"in_{name}", a.shape, _mybir.dt.from_np(a.dtype), kind="ExternalInput").ap())
    shape = arrays["in_x"].shape
    args.append(nc.dram_tensor("out_0", shape, _mybir.dt.float32, kind="ExternalOutput").ap())
    moe_lora_program(nc, *args)
    r = _run(nc, [arrays], core_ids=[0])
    return r.results[0]["out_0"]
```
